# Optimizing a Trainium2 kernel written in Bass

```python
import numpy as np
import jax
import jax.numpy as jnp

def _softmax(x, axis=-1):
    return jax.nn.softmax(x, axis=axis)

def _gelu(x):
    return jax.nn.gelu(x, approximate=True)

def _silu(x):
    return jax.nn.silu(x)

def _sigmoid(x):
    return jax.nn.sigmoid(x)

def _layernorm(x, axis=-1, eps=1e-05):
    m = jnp.mean(x, axis=axis, keepdims=True)
    v = jnp.var(x, axis=axis, keepdims=True)
    return (x - m) / jnp.sqrt(v + eps)

def _scatter_add(tgt, idx, src, axis=0):
    return tgt.at[idx].add(src)

def _segment_sum(src, seg, n):
    return jax.ops.segment_sum(src, seg, n)
kernel_name = 'mk_dlrm_tower_d1_rec_r8_925983'

def setup_inputs(seed: int=0):
    np.random.seed(seed)
    _w = jnp.asarray

    def _rec_inputs():
        import jax
        import jax.numpy as jnp
        _tk = jax.random.key(seed)
        dense_ctx = jax.random.normal(jax.random.fold_in(_tk, 190), (512, 16), jnp.float32)
        ids = jnp.stack([jax.random.randint(jax.random.fold_in(_tk, 200 + f), (512,), 0, v, jnp.int32) for f, v in enumerate([12500, 125000, 12500, 1250, 1250, 1000, 1250, 1000, 1250, 1250, 1250, 12500, 12500, 12500, 12500, 1000, 1000, 1000, 1000, 1250, 1000, 12500, 1250, 1000, 1250, 1000, 1000])], axis=1)
        tbl_0 = 0.05 * jax.random.normal(jax.random.fold_in(_tk, 500 + 0), (12500, 128), jnp.float32)
        tbl_1 = 0.05 * jax.random.normal(jax.random.fold_in(_tk, 500 + 1), (125000, 128), jnp.float32)
        tbl_2 = 0.05 * jax.random.normal(jax.random.fold_in(_tk, 500 + 2), (12500, 128), jnp.float32)
        tbl_3 = 0.05 * jax.random.normal(jax.random.fold_in(_tk, 500 + 3), (1250, 128), jnp.float32)
        tbl_4 = 0.05 * jax.random.normal(jax.random.fold_in(_tk, 500 + 4), (1250, 128), jnp.float32)
        tbl_5 = 0.05 * jax.random.normal(jax.random.fold_in(_tk, 500 + 5), (1000, 128), jnp.float32)
        tbl_6 = 0.05 * jax.random.normal(jax.random.fold_in(_tk, 500 + 6), (1250, 128), jnp.float32)
        tbl_7 = 0.05 * jax.random.normal(jax.random.fold_in(_tk, 500 + 7), (1000, 128), jnp.float32)
        tbl_8 = 0.05 * jax.random.normal(jax.random.fold_in(_tk, 500 + 8), (1250, 128), jnp.float32)
        tbl_9 = 0.05 * jax.random.normal(jax.random.fold_in(_tk, 500 + 9), (1250, 128), jnp.float32)
        tbl_10 = 0.05 * jax.random.normal(jax.random.fold_in(_tk, 500 + 10), (1250, 128), jnp.float32)
        tbl_11 = 0.05 * jax.random.normal(jax.random.fold_in(_tk, 500 + 11), (12500, 128), jnp.float32)
        tbl_12 = 0.05 * jax.random.normal(jax.random.fold_in(_tk, 500 + 12), (12500, 128), jnp.float32)
        tbl_13 = 0.05 * jax.random.normal(jax.random.fold_in(_tk, 500 + 13), (12500, 128), jnp.float32)
        tbl_14 = 0.05 * jax.random.normal(jax.random.fold_in(_tk, 500 + 14), (12500, 128), jnp.float32)
        tbl_15 = 0.05 * jax.random.normal(jax.random.fold_in(_tk, 500 + 15), (1000, 128), jnp.float32)
        tbl_16 = 0.05 * jax.random.normal(jax.random.fold_in(_tk, 500 + 16), (1000, 128), jnp.float32)
        tbl_17 = 0.05 * jax.random.normal(jax.random.fold_in(_tk, 500 + 17), (1000, 128), jnp.float32)
        tbl_18 = 0.05 * jax.random.normal(jax.random.fold_in(_tk, 500 + 18), (1000, 128), jnp.float32)
        tbl_19 = 0.05 * jax.random.normal(jax.random.fold_in(_tk, 500 + 19), (1250, 128), jnp.float32)
        tbl_20 = 0.05 * jax.random.normal(jax.random.fold_in(_tk, 500 + 20), (1000, 128), jnp.float32)
        tbl_21 = 0.05 * jax.random.normal(jax.random.fold_in(_tk, 500 + 21), (12500, 128), jnp.float32)
        tbl_22 = 0.05 * jax.random.normal(jax.random.fold_in(_tk, 500 + 22), (1250, 128), jnp.float32)
        tbl_23 = 0.05 * jax.random.normal(jax.random.fold_in(_tk, 500 + 23), (1000, 128), jnp.float32)
        tbl_24 = 0.05 * jax.random.normal(jax.random.fold_in(_tk, 500 + 24), (1250, 128), jnp.float32)
        tbl_25 = 0.05 * jax.random.normal(jax.random.fold_in(_tk, 500 + 25), (1000, 128), jnp.float32)
        tbl_26 = 0.05 * jax.random.normal(jax.random.fold_in(_tk, 500 + 26), (1000, 128), jnp.float32)
        _rk = jax.random.fold_in(_tk, 7)
        W_top1 = 0.0521996 * jax.random.normal(jax.random.fold_in(_tk, 801), (367, 512), jnp.float32)
        W_top2 = 0.0441942 * jax.random.normal(jax.random.fold_in(_tk, 802), (512, 256), jnp.float32)
        W_top3 = 0.0625 * jax.random.normal(jax.random.fold_in(_tk, 803), (256, 1), jnp.float32)
        b_top1 = jnp.zeros((512,), jnp.float32)
        b_top2 = jnp.zeros((256,), jnp.float32)
        return (dense_ctx, ids, tbl_0, tbl_1, tbl_2, tbl_3, tbl_4, tbl_5, tbl_6, tbl_7, tbl_8, tbl_9, tbl_10, tbl_11, tbl_12, tbl_13, tbl_14, tbl_15, tbl_16, tbl_17, tbl_18, tbl_19, tbl_20, tbl_21, tbl_22, tbl_23, tbl_24, tbl_25, tbl_26, W_top1, b_top1, W_top2, b_top2, W_top3)
    dense_ctx, ids, tbl_0, tbl_1, tbl_2, tbl_3, tbl_4, tbl_5, tbl_6, tbl_7, tbl_8, tbl_9, tbl_10, tbl_11, tbl_12, tbl_13, tbl_14, tbl_15, tbl_16, tbl_17, tbl_18, tbl_19, tbl_20, tbl_21, tbl_22, tbl_23, tbl_24, tbl_25, tbl_26, W_top1, b_top1, W_top2, b_top2, W_top3 = _rec_inputs()

    def _L0_rec_setup():
        import jax, jax.numpy as jnp
        import numpy as np

        def _tri_indices(num_feas):
            return np.array([i * num_feas + j for j in range(1, num_feas) for i in range(j)], dtype=np.int32)
        key = jax.random.key(seed)
        batch, num_feas, embed_dim = (2048, 27, 128)
        inputs = jax.random.normal(key, (batch, num_feas, embed_dim), dtype=jnp.float32)
        return {'inputs': inputs, 'num_feas': num_feas}
    _L0_rec_all = _L0_rec_setup()
    _L0_rec_in = {k: v for k, v in _L0_rec_all.items() if k in ()}
    del _L0_rec_all
    return {'dense_ctx': dense_ctx, 'ids': ids, 'tbl_0': tbl_0, 'tbl_1': tbl_1, 'tbl_2': tbl_2, 'tbl_3': tbl_3, 'tbl_4': tbl_4, 'tbl_5': tbl_5, 'tbl_6': tbl_6, 'tbl_7': tbl_7, 'tbl_8': tbl_8, 'tbl_9': tbl_9, 'tbl_10': tbl_10, 'tbl_11': tbl_11, 'tbl_12': tbl_12, 'tbl_13': tbl_13, 'tbl_14': tbl_14, 'tbl_15': tbl_15, 'tbl_16': tbl_16, 'tbl_17': tbl_17, 'tbl_18': tbl_18, 'tbl_19': tbl_19, 'tbl_20': tbl_20, 'tbl_21': tbl_21, 'tbl_22': tbl_22, 'tbl_23': tbl_23, 'tbl_24': tbl_24, 'tbl_25': tbl_25, 'tbl_26': tbl_26, 'W_top1': W_top1, 'b_top1': b_top1, 'W_top2': W_top2, 'b_top2': b_top2, 'W_top3': W_top3}

def reference(dense_ctx, ids, tbl_0, tbl_1, tbl_2, tbl_3, tbl_4, tbl_5, tbl_6, tbl_7, tbl_8, tbl_9, tbl_10, tbl_11, tbl_12, tbl_13, tbl_14, tbl_15, tbl_16, tbl_17, tbl_18, tbl_19, tbl_20, tbl_21, tbl_22, tbl_23, tbl_24, tbl_25, tbl_26, W_top1, b_top1, W_top2, b_top2, W_top3):
    import jax
    import jax.numpy as jnp

    def _L0_rec_ref(inputs, num_feas):
        import jax, jax.numpy as jnp
        import numpy as np

        def _tri_indices(num_feas):
            return np.array([i * num_feas + j for j in range(1, num_feas) for i in range(j)], dtype=np.int32)
        dot = jnp.einsum('bnd,bmd->bnm', inputs, inputs)
        idx = jnp.asarray(_tri_indices(num_feas))
        flat = dot.reshape(inputs.shape[0], num_feas * num_feas)
        return flat[:, idx]
    e = jnp.stack([tbl_0[ids[:, 0]], tbl_1[ids[:, 1]], tbl_2[ids[:, 2]], tbl_3[ids[:, 3]], tbl_4[ids[:, 4]], tbl_5[ids[:, 5]], tbl_6[ids[:, 6]], tbl_7[ids[:, 7]], tbl_8[ids[:, 8]], tbl_9[ids[:, 9]], tbl_10[ids[:, 10]], tbl_11[ids[:, 11]], tbl_12[ids[:, 12]], tbl_13[ids[:, 13]], tbl_14[ids[:, 14]], tbl_15[ids[:, 15]], tbl_16[ids[:, 16]], tbl_17[ids[:, 17]], tbl_18[ids[:, 18]], tbl_19[ids[:, 19]], tbl_20[ids[:, 20]], tbl_21[ids[:, 21]], tbl_22[ids[:, 22]], tbl_23[ids[:, 23]], tbl_24[ids[:, 24]], tbl_25[ids[:, 25]], tbl_26[ids[:, 26]]], axis=1)
    z = _L0_rec_ref(e, 27)
    z = z.reshape(z.shape[0], -1)
    h = jnp.concatenate([z, dense_ctx], axis=1)
    h = jnp.maximum(h @ W_top1 + b_top1, 0.0)
    h = jnp.maximum(h @ W_top2 + b_top2, 0.0)
    y = h @ W_top3
    return y

_drawn_inputs = setup_inputs


def setup_inputs(seed=0):
    import zlib

    import numpy as np

    out = dict(_drawn_inputs(seed))
    spreads = {'b_top1': (0.0, 0.1), 'b_top2': (0.0, 0.1)}
    factors = {}
    for name, (base, spread) in spreads.items():
        noise = np.random.default_rng([zlib.crc32(name.encode()), seed]).standard_normal(out[name].shape)
        drawn = base * np.exp(spread * noise) if base else spread * noise
        out[name] = jnp.asarray(drawn.astype(out[name].dtype))
    for name, factor in factors.items():
        out[name] = (out[name] * factor).astype(out[name].dtype)
    return out
```

```python
from contextlib import ExitStack

import numpy as np
import concourse.bass as bass
from concourse import mybir

F32 = mybir.dt.float32
F16 = mybir.dt.float16
BF16 = mybir.dt.bfloat16
U32 = mybir.dt.uint32
ALU = mybir.AluOpType
ACT = mybir.ActivationFunctionType

P = 128
Q = 32
NQ = P // Q
BANK = 512
ONE_HOT_VOCAB = 1000
MAX_ONE_HOT = 8
VP = 125
VQ = ONE_HOT_VOCAB // VP
FULL_DMA = VP // 16 * 16


def pair_groups(nf, nd):
    groups, j1, extra = [], nf, nd
    while j1 > 1:
        w = j1 - 1
        rows = min((P - extra) // w, j1 - 1)
        groups.append((j1 - rows, j1, w))
        j1 -= rows
        extra = 0
    return groups[::-1]


def runs(features):
    out = []
    for i, f in enumerate(features):
        if out and out[-1][1] + out[-1][2] == f:
            out[-1][2] += 1
        else:
            out.append([i, f, 1])
    return out


def build(nc, dense_ctx, ids, tables, w_top1, b_top1, w_top2, b_top2, w_top3, consts, y):
    B, NF = ids.shape
    D = tables[0].shape[1]
    ND = dense_ctx.shape[1]
    N1, N2 = w_top1.shape[1], w_top2.shape[1]
    M1, M2 = N1 // P, N2 // P
    CH = B // P
    assert D == P and NF <= Q 

    one_hot = [f for f in range(NF) if tables[f].shape[0] == ONE_HOT_VOCAB][-MAX_ONE_HOT:]
    gathered = [f for f in range(NF) if f not in one_hot]
    NO, NG = len(one_hot), len(gathered)
    batches = [gathered[i:i + BANK // P] for i in range(0, NG, BANK // P)]
    NB = len(batches)
    groups = pair_groups(NF, ND)
    GP = [(j1 - j0) * w for j0, j1, w in groups]
    GK = GP[:-1] + [GP[-1] + ND]
    spb = Q // 2
    assert spb * NF <= BANK and len(groups) * P <= BANK

    with ExitStack() as ctx:
        def sb(name, shape, dt=F32):
            return ctx.enter_context(nc.sbuf_tensor(name, shape, dt))

        def psum(name, shape):
            return ctx.enter_context(nc.psum_tensor(name, shape, F32))

        def sem(name):
            return ctx.enter_context(nc.semaphore(name))

        cst = sb("cst", [P, P + VQ])
        ident, row_no = cst[:, 0:P], cst[:, P:P + VQ]
        ids_sb = sb("ids_sb", [P, CH, NF], ids.dtype)
        ids_f = sb("ids_f", [P, CH, NF])
        ids_t = sb("ids_t", [NF, B])
        emb = sb("emb", [P, CH, NG, D])
        emb_t = sb("emb_t", [P, B, NF])
        table = sb("table", [P, NO, VQ, D])
        parts = sb("parts", [P, 2, 3, VQ, D], BF16)
        id_row = sb("id_row", [P, 2, B], F16)
        hot = sb("hot", [P, 2, VQ, B], BF16)
        z = sb("z", [P, 2, NF, Q])
        zc = sb("zc", [P, CH, len(groups), P])
        zt = sb("zt", [P, len(groups), B])
        w1 = sb("w1", [P, len(groups), N1])
        w2 = sb("w2", [P, M1, N2])
        w3 = sb("w3", [P, M2])
        b1 = sb("b1", [P, M1])
        b2 = sb("b2", [P, M2])
        h1 = sb("h1", [P, M1, B])
        h2 = sb("h2", [P, M2, B])
        y_row = sb("y_row", [1, B])

        ps_emb = psum("ps_emb", [P, 2, BANK])
        ps_gram = psum("ps_gram", [P, 2, BANK])
        ps_z = psum("ps_z", [P, BANK])
        ps_acc = psum("ps_acc", [P, 2, BANK])

        ids_in = sem("ids_in")
        cst_in = sem("cst_in")
        dense_in = sem("dense_in")
        w_in = sem("w_in")
        table_in = [sem(f"table_in{n}") for n in range(NO)]
        rows_in = [[sem(f"rows_in{c}_{i}") for i in range(NB)] for c in range(CH)]
        y_out = sem("y_out")
        w1_zero = sem("w1_zero")
        init_done = sem("init_done")
        ids_f_ready = sem("ids_f_ready")
        ids_t_done = sem("ids_t_done")
        ids_t_ready = sem("ids_t_ready")
        bcast_done = sem("bcast_done")
        id_row_ready = sem("id_row_ready")
        act_part = sem("act_part")
        dve_part = sem("dve_part")
        hot_ready = sem("hot_ready")
        acc_done = sem("acc_done")
        acc_read = sem("acc_read")
        emb_tr = sem("emb_tr")
        emb_read = [sem("emb_read_dve"), sem("emb_read_act")]
        gram_done = sem("gram_done")
        z_ready = sem("z_ready")
        zc_dve = sem("zc_dve")
        zc_act = sem("zc_act")
        zt_done = sem("zt_done")
        zt_ready = sem("zt_ready")

        ranges = [(0, (CH - 1) * P), ((CH - 1) * P, B)]
        USES = M1 + M2 + 1
        half = (len(groups) + 1) // 2

        def weight_count():
            return 16 * (NF + 4)

        block = ctx.enter_context(nc.Block())

        @block.sync
        def _(sp):
            sp.dma_start(ids_sb[:], ids.rearrange("(c p) f -> p c f", p=P)).then_inc(ids_in, 16)
            for n, f in enumerate(one_hot):
                src = tables[f].rearrange("(p q) d -> p q d", q=VQ)
                for a, b in ((0, FULL_DMA), (FULL_DMA, VP)):
                    sp.dma_start(table[a:b, n], src[a:b]).then_inc(table_in[n], 16)
            sp.dma_start(zc[:, :, len(groups) - 1, GP[-1]:GK[-1]], dense_ctx.rearrange("(c p) e -> p c e", p=P)
                         ).then_inc(dense_in, 16)
            with nc.allow_non_contiguous_dma(reason="biases and last weights, one value per partition"):
                sp.dma_start(b1[:], b_top1.rearrange("(m p) -> p m", p=P)).then_inc(w_in, 16)
                sp.dma_start(b2[:], b_top2.rearrange("(m p) -> p m", p=P)).then_inc(w_in, 16)
                sp.dma_start(w3[:], w_top3.rearrange("(m p) o -> p (m o)", p=P)).then_inc(w_in, 16)
            sp.dma_start(w2[:], w_top2.rearrange("(m p) n -> p m n", p=P)).then_inc(w_in, 16)
            sp.wait_ge(w1_zero, 1)
            for g, (j0, j1, w) in enumerate(groups):
                for j in range(j0, j1):
                    at, first = (j - j0) * w, j * (j - 1) // 2
                    sp.dma_start(w1[at:at + j, g, :], w_top1[first:first + j, :]).then_inc(w_in, 16)
            sp.dma_start(w1[GP[-1]:GK[-1], len(groups) - 1, :], w_top1[NF * (NF - 1) // 2:, :]).then_inc(w_in, 16)
            for r, (b0, bn) in enumerate(ranges):
                sp.wait_ge(acc_read, NO + USES * (r + 1))
                sp.dma_start(y[b0:bn, :].rearrange("b o -> o b"), y_row[0:1, b0:bn]).then_inc(y_out, 16)
            sp.wait_ge(y_out, 16 * len(ranges))

        @block.gpsimd
        def _(pool):
            pool.wait_ge(ids_in, 16)
            for c in range(CH):
                for i, batch in enumerate(batches):
                    for s, f in enumerate(batch):
                        index = ids_sb[:, c, f:f + 1].bitcast(U32)
                        pool.indirect_dma_start(emb[:, c, i * (BANK // P) + s, :], None, tables[f],
                                                bass.IndirectOffsetOnAxis(ap=index, axis=0)
                                                ).then_inc(rows_in[c][i], 16)

        def emb_t_copy(eng_copy, c, i):
            src = ps_emb[:, (c * NB + i) % 2, :].rearrange("p (f b) -> p b f", b=P)
            for at, f, n in runs(batches[i]):
                last = eng_copy(emb_t[:, c * P:(c + 1) * P, f:f + n], src[:, :, at:at + n])
            return last

        def compact(eng_copy, c, g):
            j0, j1, w = groups[g]
            return eng_copy(zc[:, c, g, 0:GP[g]].rearrange("p (j i) -> p j i", i=w), z[:, c % 2, j0:j1, 0:w])

        @block.tensor
        def _(pe):
            def turn_ids():
                pe.wait_ge(cst_in, 16)
                pe.wait_ge(init_done, 1)
                pe.wait_ge(ids_f_ready, 1)
                for c in range(CH):
                    last = pe.transpose(ps_z[0:NF, c * P:(c + 1) * P], ids_f[:, c, :], ident)
                last.then_inc(ids_t_done, 1)

            def broadcast_ids(n):
                pe.wait_ge(ids_t_ready, 1)
                if n:
                    pe.wait_ge(id_row_ready, n)
                f = one_hot[n]
                pe.matmul(ps_z[:, 0:B], ident[0:NF, f:f + 1].to_broadcast([NF, P]), ids_t[:, :],
                          start=True, stop=True).then_inc(bcast_done, 1)

            def look_up(n):
                pe.wait_ge(dve_part, 2 * n + 2)
                pe.wait_ge(hot_ready, n + 1)
                if n >= 2:
                    pe.wait_ge(acc_read, n - 1)
                for q in range(VQ):
                    for part in range(3):
                        last = pe.matmul(ps_acc[:, n % 2, 0:B], parts[0:VP, n % 2, part, q, :], hot[0:VP, n % 2, q, :],
                                         start=(q == 0 and part == 0), stop=(q == VQ - 1 and part == 2))
                last.then_inc(acc_done, 1)

            def turn_rows(c, i):
                t = c * NB + i
                pe.wait_ge(cst_in, 16)
                pe.wait_ge(rows_in[c][i], 16 * len(batches[i]))
                if t >= 2:
                    pe.wait_ge(emb_read[t % 2], t // 2)
                for s in range(len(batches[i])):
                    last = pe.transpose(ps_emb[:, t % 2, s * P:(s + 1) * P], emb[:, c, i * (BANK // P) + s, :], ident)
                last.then_inc(emb_tr, 1)

            def gram(c):
                if c == 0:
                    pe.wait_ge(init_done, 2)
                    pe.wait_ge(acc_read, NO)
                else:
                    pe.wait_ge(z_ready, c)
                done = (c + 1) * NB
                pe.wait_ge(emb_read[0], (done + 1) // 2)
                pe.wait_ge(emb_read[1], done // 2)
                for s in range(Q):
                    for k in range(NQ):
                        e = emb_t[:, c * P + k * Q + s, :]
                        out = ps_gram[k * Q:k * Q + NF, s // spb, s % spb * NF:(s % spb + 1) * NF]
                        last = pe.matmul(out, e, e, start=True, stop=True, tile_position=(0, k * Q))
                last.then_inc(gram_done, 1)

            def turn_products(c):
                pe.wait_ge(zc_dve, c + 1)
                pe.wait_ge(zc_act, c + 1)
                if c == 0:
                    pe.wait_ge(dense_in, 16)
                    pe.wait_ge(id_row_ready, NO)
                else:
                    pe.wait_ge(zt_ready, c)
                for g in range(len(groups)):
                    last = pe.transpose(ps_z[0:GK[g], g * P:(g + 1) * P], zc[:, c, g, 0:GK[g]], ident)
                last.then_inc(zt_done, 1)

            def dense_layers(r):
                b0, bn = ranges[r]
                n = bn - b0
                u = NO + USES * r
                pe.wait_ge(w_in, weight_count())
                pe.wait_ge(zt_ready, bn // P)
                for m in range(M1):
                    if u >= 2:
                        pe.wait_ge(acc_read, u - 1)
                    for g in range(len(groups)):
                        last = pe.matmul(ps_acc[:, u % 2, 0:n], w1[0:GK[g], g, m * P:(m + 1) * P], zt[0:GK[g], g, b0:bn],
                                         start=(g == 0), stop=(g == len(groups) - 1))
                    last.then_inc(acc_done, 1)
                    u += 1
                for m2 in range(M2):
                    pe.wait_ge(acc_read, u - 1)
                    for m in range(M1):
                        if m2 == 0:
                            pe.wait_ge(acc_read, NO + USES * r + m + 1)
                        last = pe.matmul(ps_acc[:, u % 2, 0:n], w2[:, m, m2 * P:(m2 + 1) * P], h1[:, m, b0:bn],
                                         start=(m == 0), stop=(m == M1 - 1))
                    last.then_inc(acc_done, 1)
                    u += 1
                for m2 in range(M2):
                    pe.wait_ge(acc_read, NO + USES * r + M1 + m2 + 1)
                    last = pe.matmul(ps_acc[0:1, u % 2, 0:n], w3[:, m2:m2 + 1], h2[:, m2, b0:bn],
                                     start=(m2 == 0), stop=(m2 == M2 - 1))
                last.then_inc(acc_done, 1)

            turn_ids()
            if NO:
                broadcast_ids(0)
            for n in range(NO):
                if n + 1 < NO:
                    broadcast_ids(n + 1)
                look_up(n)
                if n == NO // 2 - 1:
                    for i in range(NB):
                        turn_rows(0, i)
            for i in range(NB):
                turn_rows(1, i)
            gram(0)
            gram(1)
            turn_products(0)
            for i in range(NB):
                turn_rows(2, i)
            turn_products(1)
            gram(2)
            turn_products(2)
            dense_layers(0)
            for i in range(NB):
                turn_rows(3, i)
            gram(3)
            turn_products(3)
            dense_layers(1)

        @block.vector
        def _(dve):
            def split(n):
                for a in range(2):
                    dve.wait_ge(act_part, 2 * n + a + 1)
                    if a == 0:
                        out = table[0:VP, n]
                    else:
                        out = parts[0:VP, n % 2, 2]
                    dve.tensor_tensor(out, table[0:VP, n], parts[0:VP, n % 2, a], ALU.subtract).then_inc(dve_part, 1)

            def make_hot(n):
                dve.wait_ge(id_row_ready, n + 1)
                if n == 0:
                    dve.wait_ge(cst_in, 16)
                if n >= 2:
                    dve.wait_ge(acc_done, n - 1)
                for q in range(VQ):
                    last = dve.tensor_scalar(hot[0:VP, n % 2, q, :], id_row[0:VP, n % 2, :], row_no[0:VP, q:q + 1], None,
                                             ALU.is_equal)
                last.then_inc(hot_ready, 1)

            def copy_batches(c):
                for i in range(NB):
                    t = c * NB + i
                    if t % 2 == 0:
                        dve.wait_ge(emb_tr, t + 1)
                        emb_t_copy(dve.tensor_copy, c, i).then_inc(emb_read[0], 1)

            def products(c):
                dve.wait_ge(gram_done, c + 1)
                if c >= 2:
                    dve.wait_ge(zc_act, c - 1)
                src = ps_gram[:, :, 0:spb * NF].rearrange("p h (s j) -> p j h s", j=NF)
                dve.transpose(z[:, c % 2, 1:NF, :], src[:, 1:NF]).then_inc(z_ready, 1)
                dve.wait_ge(z_ready, c + 1)
                for g in range(half):
                    last = compact(dve.tensor_copy, c, g)
                last.then_inc(zc_dve, 1)

            def copy_zt(c):
                dve.wait_ge(zt_done, c + 1)
                rows = max(GK)
                dve.tensor_copy(zt[0:rows, :, c * P:(c + 1) * P],
                                ps_z[0:rows, :].rearrange("p (g b) -> p g b", b=P)).then_inc(zt_ready, 1)

            dve.memset(w1[:], 0.0).then_inc(w1_zero, 1)
            dve.memset(ps_z[:], 0.0).then_inc(init_done, 1)
            dve.wait_ge(ids_in, 16)
            dve.tensor_copy(ids_f[:], ids_sb[:]).then_inc(ids_f_ready, 1)
            dve.memset(ps_gram[:], 0.0).then_inc(init_done, 1)
            dve.wait_ge(ids_t_done, 1)
            dve.tensor_copy(ids_t[:], ps_z[0:NF, 0:B]).then_inc(ids_t_ready, 1)
            for n in range(NO):
                split(n)
                make_hot(n)
                if n == NO // 2:
                    copy_batches(0)
            copy_batches(1)
            products(0)
            products(1)
            copy_zt(0)
            copy_batches(2)
            copy_zt(1)
            products(2)
            copy_zt(2)
            copy_batches(3)
            products(3)
            copy_zt(3)

        @block.scalar
        def _(act):
            def copy(out, in_):
                return act.activation(out, in_, ACT.Copy)

            def first_parts(n):
                act.wait_ge(table_in[n], 32)
                if n >= 2:
                    act.wait_ge(acc_done, n - 1)
                copy(parts[0:VP, n % 2, 0], table[0:VP, n]).then_inc(act_part, 1)
                act.wait_ge(dve_part, 2 * n + 1)
                copy(parts[0:VP, n % 2, 1], table[0:VP, n]).then_inc(act_part, 1)

            def copy_id_row(n):
                act.wait_ge(bcast_done, n + 1)
                if n >= 2:
                    act.wait_ge(hot_ready, n - 1)
                copy(id_row[:, n % 2, :], ps_z[:, 0:B]).then_inc(id_row_ready, 1)

            def looked_up(n):
                act.wait_ge(acc_done, n + 1)
                copy(emb_t[:, :, one_hot[n]], ps_acc[:, n % 2, 0:B]).then_inc(acc_read, 1)

            def copy_batches(c):
                for i in range(NB):
                    t = c * NB + i
                    if t % 2 == 1:
                        act.wait_ge(emb_tr, t + 1)
                        emb_t_copy(copy, c, i).then_inc(emb_read[1], 1)

            def compact_products(c):
                act.wait_ge(z_ready, c + 1)
                for g in range(half, len(groups)):
                    last = compact(copy, c, g)
                last.then_inc(zc_act, 1)

            def dense_layers(r):
                b0, bn = ranges[r]
                n = bn - b0
                u = NO + USES * r
                if r == 0:
                    act.wait_ge(w_in, weight_count())
                for m in range(M1):
                    act.wait_ge(acc_done, u + 1)
                    act.activation(h1[:, m, b0:bn], ps_acc[:, u % 2, 0:n], ACT.Relu,
                                   bias=b1[:, m:m + 1]).then_inc(acc_read, 1)
                    u += 1
                for m2 in range(M2):
                    act.wait_ge(acc_done, u + 1)
                    act.activation(h2[:, m2, b0:bn], ps_acc[:, u % 2, 0:n], ACT.Relu,
                                   bias=b2[:, m2:m2 + 1]).then_inc(acc_read, 1)
                    u += 1
                act.wait_ge(acc_done, u + 1)
                copy(y_row[0:1, b0:bn], ps_acc[0:1, u % 2, 0:n]).then_inc(acc_read, 1)

            act.dma_start(cst[:], consts).then_inc(cst_in, 16)
            if NO:
                first_parts(0)
                copy_id_row(0)
            for n in range(NO):
                if n + 1 < NO:
                    copy_id_row(n + 1)
                    first_parts(n + 1)
                looked_up(n)
                if n == NO // 2 - 1:
                    copy_batches(0)
            copy_batches(1)
            compact_products(0)
            compact_products(1)
            copy_batches(2)
            compact_products(2)
            dense_layers(0)
            copy_batches(3)
            compact_products(3)
            dense_layers(1)


N_TABLES = 27
_INS = ["dense_ctx", "ids"] + [f"tbl_{f}" for f in range(N_TABLES)] + ["W_top1", "b_top1", "W_top2", "b_top2", "W_top3"]


def kernel(**inputs):
    import numpy as _np
    import concourse.bacc as _bacc
    from concourse import mybir as _mybir
    from concourse.bass_utils import run_bass_kernel_spmd as _run

    nc = _bacc.Bacc("TRN2", target_bir_lowering=False, num_devices=1)
    arrays, aps = {}, {}

    def give(name, a):
        arrays[f"in_{name}"] = a
        aps[name] = nc.dram_tensor(f"in_{name}", a.shape, _mybir.dt.from_np(a.dtype), kind="ExternalInput").ap()

    for name in _INS:
        give(name, _np.ascontiguousarray(inputs[name]))
    give("consts", _np.concatenate([_np.eye(P, dtype=_np.float32),
                                    _np.arange(P * VQ, dtype=_np.float32).reshape(P, VQ)], axis=1))
    batch = inputs["ids"].shape[0]
    y = nc.dram_tensor("out_y", (batch, 1), _mybir.dt.float32, kind="ExternalOutput").ap()
    build(nc, aps["dense_ctx"], aps["ids"], [aps[f"tbl_{f}"] for f in range(N_TABLES)], aps["W_top1"], aps["b_top1"],
          aps["W_top2"], aps["b_top2"], aps["W_top3"], aps["consts"], y)
    r = _run(nc, [arrays], core_ids=[0])
    return r.results[0]["out_y"]
```

```python
from contextlib import ExitStack

import numpy as np
import concourse.bass as bass
from concourse import mybir

F32 = mybir.dt.float32
F16 = mybir.dt.float16
F32R = mybir.dt.float32r
U32 = mybir.dt.uint32
ALU = mybir.AluOpType
ACT = mybir.ActivationFunctionType

P = 128
Q = 32
NQ = P // Q
BANK = 512
ONE_HOT_VOCAB = 1000
F16_EXACT = 2048.0
MAX_ONE_HOT = 9
VP = 125
VQ = ONE_HOT_VOCAB // VP
TR = 3
ACT_FIRST = 10
PR = 3
ER = 3
IR = 4
FULL_DMA = VP // 16 * 16


def pair_blocks(nf, spare):
    blocks, j = [], 1
    while j < nf:
        rows = min(2, nf - j)
        if rows + 1 <= nf - j and spare - 3 >= (nf - j - 3 + 1) // 2:
            rows = 3
        spare -= rows * (rows - 1) // 2
        blocks.append((j, j + rows, j + rows - 1))
        j += rows
    assert spare >= 0
    return blocks


def runs(features):
    out = []
    for i, f in enumerate(features):
        if out and out[-1][1] + out[-1][2] == f:
            out[-1][2] += 1
        else:
            out.append([i, f, 1])
    return out


def build(nc, dense_ctx, ids, tables, w_top1, b_top1, w_top2, b_top2, w_top3, consts, y):
    B, NF = ids.shape
    D = tables[0].shape[1]
    ND = dense_ctx.shape[1]
    N1, N2 = w_top1.shape[1], w_top2.shape[1]
    M1, M2 = N1 // P, N2 // P
    CH = B // P
    assert D == P and NF <= Q 

    one_hot = [f for f in range(NF) if tables[f].shape[0] == ONE_HOT_VOCAB][-MAX_ONE_HOT:]
    gathered = [f for f in range(NF) if f not in one_hot]
    NO, NG = len(one_hot), len(gathered)
    batches = [gathered[i:i + BANK // P] for i in range(0, NG, BANK // P)]
    NB = len(batches)
    pairs = NF * (NF - 1) // 2
    KT = -(-(pairs + ND) // P)
    blocks = pair_blocks(NF, KT * P - pairs - ND)
    starts = [sum((j1 - j0) * w for j0, j1, w in blocks[:n]) for n in range(len(blocks) + 1)]
    K1 = starts[-1] + ND
    tiles = [(g * P, min((g + 1) * P, K1)) for g in range(KT)]
    spb = Q // 2
    assert spb * NF <= BANK and KT * P <= BANK and len(tiles) == KT

    with ExitStack() as ctx:
        def sb(name, shape, dt=F32):
            return ctx.enter_context(nc.sbuf_tensor(name, shape, dt))

        def psum(name, shape):
            return ctx.enter_context(nc.psum_tensor(name, shape, F32))

        def sem(name):
            return ctx.enter_context(nc.semaphore(name))

        cst = sb("cst", [P, P + VQ])
        ident, row_no = cst[:, 0:P], cst[:, P:P + VQ]
        ids_sb = sb("ids_sb", [P, CH, NF], ids.dtype)
        ids_f = sb("ids_f", [P, CH, NF])
        ids_t = sb("ids_t", [NF, B], F16)
        ident16 = sb("ident16", [NF, NF], F16)
        emb = sb("emb", [P, ER, NG, D])
        emb_t = sb("emb_t", [P, B, NF])
        table = sb("table", [P, TR, VQ, D])
        hi = sb("hi", [P, PR, VQ, D], F32R)
        lo = sb("lo", [P, PR, VQ, D], F32R)
        id_row = sb("id_row", [P, IR, B])
        hot = sb("hot", [P, 2, VQ, B], F32R)
        z = sb("z", [P, 2, NF, Q])
        zc = sb("zc", [P, CH, KT * P])
        zt = sb("zt", [P, KT, B])
        w1 = sb("w1", [P, KT, N1])
        w2 = sb("w2", [P, M1, N2])
        w3 = sb("w3", [P, M2])
        b1 = sb("b1", [P, M1])
        b2 = sb("b2", [P, M2])
        h1 = sb("h1", [P, M1, B])
        h2 = sb("h2", [P, M2, B])
        y_row = sb("y_row", [1, B])

        ps_emb = psum("ps_emb", [P, 2, BANK])
        ps_gram = psum("ps_gram", [P, 2, BANK])
        ps_z = psum("ps_z", [P, BANK])
        ps_acc = psum("ps_acc", [P, 2, BANK])

        ids_in = sem("ids_in")
        cst_in = sem("cst_in")
        dense_in = sem("dense_in")
        w_in = sem("w_in")
        table_in = [sem(f"table_in{n}") for n in range(NO)]
        rows_in = [[sem(f"rows_in{c}_{i}") for i in range(NB)] for c in range(CH)]
        y_out = sem("y_out")
        w1_zero = sem("w1_zero")
        init_done = sem("init_done")
        ids_f_ready = sem("ids_f_ready")
        ids_t_done = sem("ids_t_done")
        ids_t_ready = sem("ids_t_ready")
        bcast_done = sem("bcast_done")
        id_row_ready = sem("id_row_ready")
        hi_ready = sem("hi_ready")
        lo_ready = sem("lo_ready")
        hot_ready = sem("hot_ready")
        acc_done = sem("acc_done")
        acc_read = sem("acc_read")
        emb_tr = sem("emb_tr")
        emb_read = [sem("emb_read_dve"), sem("emb_read_act")]
        gram_done = sem("gram_done")
        z_ready = sem("z_ready")
        zc_dve = sem("zc_dve")
        zc_act = sem("zc_act")
        zt_done = sem("zt_done")
        zt_ready = sem("zt_ready")

        ranges = [(0, 2 * P), (2 * P, 3 * P), (3 * P, 4 * P)]
        USES = M1 + M2 + 1
        mine = {"dve": range(0, len(blocks) * 2 // 3), "act": range(len(blocks) * 2 // 3, len(blocks))}

        w1_rows = []
        for at, (j0, j1, w) in zip(starts, blocks):
            w1_rows += [(at + (j - j0) * w, j * (j - 1) // 2, j) for j in range(j0, j1)]
        w1_rows.append((starts[-1], pairs, ND))
        w1_rows = [(max(at, a), first + max(at, a) - at, min(at + n, b) - max(at, a))
                   for at, first, n in w1_rows for a, b in tiles if at < b and at + n > a]

        steps = []
        def prepare(n, what):
            if n < NO:
                steps.append((what, n))
        def turns(c, i0=0, i1=NB):
            steps.extend(("turn", c, i) for i in range(i0, min(i1, NB)))
        steps += [("parts", 0), ("ids", 0), ("hot", 0), ("parts", 1), ("ids", 1), ("hot", 1), ("ids", 2)]
        tn = 0
        for n in range(NO):
            if n + 3 < NO:
                steps.append(("ids", n + 3))
            prepare(n + 2, "parts")
            steps.append(("look", n))
            prepare(n + 2, "hot")
            if n >= 2:
                turns(tn // NB, tn % NB, tn % NB + 1)
                tn += 1
        turns(tn // NB, tn % NB)
        if tn < NB:
            turns(1)
        steps += [("gram", 0), ("products", 0), ("gram", 1), ("zt", 0), ("products", 1), ("turn", 2, 0), ("turn", 2, 1),
                  ("zt", 1), ("dense", 0), ("later", 0)]
        turns(2, 2)
        steps += [("gram", 2), ("products", 2), ("turn", 3, 0), ("turn", 3, 1), ("zt", 2), ("dense", 1)]
        turns(3, 2)
        steps += [("gram", 3), ("products", 3), ("later", 1), ("zt", 3), ("dense", 2), ("later", 2)]

        def copier(t):
            return 1 if t < ACT_FIRST or t % 2 else 0

        def copies(t, who):
            return sum(copier(x) == who for x in range(t))

        weight_count = 16 * (len(w1_rows) + 4)

        block = ctx.enter_context(nc.Block())

        @block.sync
        def _(sp):
            sp.dma_start(ids_sb[:], ids.rearrange("(c p) f -> p c f", p=P)).then_inc(ids_in, 16)
            for n, f in enumerate(one_hot):
                if n >= TR:
                    sp.wait_ge(lo_ready, n - TR + 1)
                src = tables[f].rearrange("(p q) d -> p q d", q=VQ)
                for a, b in ((0, FULL_DMA), (FULL_DMA, VP)):
                    sp.dma_start(table[a:b, n % TR], src[a:b]).then_inc(table_in[n], 16)
            sp.dma_start(zc[:, :, starts[-1]:K1], dense_ctx.rearrange("(c p) e -> p c e", p=P)
                         ).then_inc(dense_in, 16)
            with nc.allow_non_contiguous_dma(reason="biases and last weights, one value per partition"):
                sp.dma_start(b1[:], b_top1.rearrange("(m p) -> p m", p=P)).then_inc(w_in, 16)
                sp.dma_start(b2[:], b_top2.rearrange("(m p) -> p m", p=P)).then_inc(w_in, 16)
                sp.dma_start(w3[:], w_top3.rearrange("(m p) o -> p (m o)", p=P)).then_inc(w_in, 16)
            sp.dma_start(w2[:], w_top2.rearrange("(m p) n -> p m n", p=P)).then_inc(w_in, 16)
            sp.wait_ge(w1_zero, 1)
            for at, first, n in w1_rows:
                g, p0 = at // P, at % P
                sp.dma_start(w1[p0:p0 + n, g, :], w_top1[first:first + n, :]).then_inc(w_in, 16)
            for r, (b0, bn) in enumerate(ranges):
                sp.wait_ge(acc_read, NO + USES * (r + 1))
                sp.dma_start(y[b0:bn, :].rearrange("b o -> o b"), y_row[0:1, b0:bn]).then_inc(y_out, 16)
            sp.wait_ge(y_out, 16 * len(ranges))

        @block.gpsimd
        def _(pool):
            pool.memset(w1[:], 0.0).then_inc(w1_zero, 1)
            pool.wait_ge(ids_in, 16)
            for c in range(CH):
                for i, batch in enumerate(batches):
                    if c >= ER:
                        pool.wait_ge(emb_tr, (c - ER) * NB + i + 1)
                    for s, f in enumerate(batch):
                        index = ids_sb[:, c, f:f + 1].bitcast(U32)
                        pool.indirect_dma_start(emb[:, c % ER, i * (BANK // P) + s, :], None, tables[f],
                                                bass.IndirectOffsetOnAxis(ap=index, axis=0)
                                                ).then_inc(rows_in[c][i], 16)

        def emb_t_copy(eng_copy, c, i):
            src = ps_emb[:, (c * NB + i) % 2, :].rearrange("p (f b) -> p b f", b=P)
            for at, f, n in runs(batches[i]):
                last = eng_copy(emb_t[:, c * P:(c + 1) * P, f:f + n], src[:, :, at:at + n])
            return last

        def compact(eng_copy, c, n):
            j0, j1, w = blocks[n]
            return eng_copy(zc[:, c, starts[n]:starts[n + 1]].rearrange("p (j i) -> p j i", i=w), z[:, c % 2, j0:j1, 0:w])

        @block.tensor
        def _(pe):
            def turn_ids():
                pe.wait_ge(cst_in, 16)
                pe.wait_ge(init_done, 1)
                pe.wait_ge(ids_f_ready, 1)
                for c in range(CH):
                    last = pe.transpose(ps_z[0:NF, c * P:(c + 1) * P], ids_f[:, c, :], ident)
                last.then_inc(ids_t_done, 1)

            def broadcast_ids(n):
                pe.wait_ge(ids_t_ready, 1)
                if n:
                    pe.wait_ge(id_row_ready, n)
                f = one_hot[n]
                pe.matmul(ps_z[:, 0:B], ident16[:, f:f + 1].to_broadcast([NF, P]), ids_t[:, :],
                          start=True, stop=True).then_inc(bcast_done, 1)

            def look_up(n):
                pe.wait_ge(lo_ready, n + 1)
                pe.wait_ge(hot_ready, n + 1)
                if n >= 2:
                    pe.wait_ge(acc_read, n - 1)
                for q in range(VQ):
                    for part in (hi, lo):
                        last = pe.matmul(ps_acc[:, n % 2, 0:B], part[0:VP, n % PR, q, :], hot[0:VP, n % 2, q, :],
                                         start=(q == 0 and part is hi), stop=(q == VQ - 1 and part is lo))
                last.then_inc(acc_done, 1)

            def turn_rows(c, i):
                t = c * NB + i
                pe.wait_ge(cst_in, 16)
                pe.wait_ge(rows_in[c][i], 16 * len(batches[i]))
                if t >= 2:
                    pe.wait_ge(emb_read[copier(t - 2)], copies(t - 1, copier(t - 2)))
                for s in range(len(batches[i])):
                    last = pe.transpose(ps_emb[:, t % 2, s * P:(s + 1) * P], emb[:, c % ER, i * (BANK // P) + s, :], ident)
                last.then_inc(emb_tr, 1)

            def gram(c):
                if c == 0:
                    pe.wait_ge(init_done, 2)
                    pe.wait_ge(acc_read, NO)
                else:
                    pe.wait_ge(z_ready, c)
                for who in range(2):
                    if copies((c + 1) * NB, who):
                        pe.wait_ge(emb_read[who], copies((c + 1) * NB, who))
                for s in range(Q):
                    for k in range(NQ):
                        e = emb_t[:, c * P + k * Q + s, :]
                        out = ps_gram[k * Q:k * Q + NF, s // spb, s % spb * NF:(s % spb + 1) * NF]
                        last = pe.matmul(out, e, e, start=True, stop=True, tile_position=(0, k * Q))
                last.then_inc(gram_done, 1)

            def turn_products(c):
                pe.wait_ge(zc_dve, c + 1)
                pe.wait_ge(zc_act, c + 1)
                if c == 0:
                    pe.wait_ge(dense_in, 16)
                    pe.wait_ge(id_row_ready, NO)
                else:
                    pe.wait_ge(zt_ready, c)
                for g, (a, b) in enumerate(tiles):
                    last = pe.transpose(ps_z[0:b - a, g * P:(g + 1) * P], zc[:, c, a:b], ident)
                last.then_inc(zt_done, 1)

            def first_layer(r):
                b0, bn = ranges[r]
                n = bn - b0
                u = NO + USES * r
                pe.wait_ge(w_in, weight_count)
                pe.wait_ge(zt_ready, bn // P)
                for m in range(M1):
                    if u >= 2:
                        pe.wait_ge(acc_read, u - 1)
                    for g, (a, b) in enumerate(tiles):
                        last = pe.matmul(ps_acc[:, u % 2, 0:n], w1[0:b - a, g, m * P:(m + 1) * P], zt[0:b - a, g, b0:bn],
                                         start=(g == 0), stop=(g == KT - 1))
                    last.then_inc(acc_done, 1)
                    u += 1

            def later_layers(r):
                b0, bn = ranges[r]
                n = bn - b0
                u = NO + USES * r + M1
                for m2 in range(M2):
                    pe.wait_ge(acc_read, u - 1)
                    for m in range(M1):
                        if m2 == 0:
                            pe.wait_ge(acc_read, NO + USES * r + m + 1)
                        last = pe.matmul(ps_acc[:, u % 2, 0:n], w2[:, m, m2 * P:(m2 + 1) * P], h1[:, m, b0:bn],
                                         start=(m == 0), stop=(m == M1 - 1))
                    last.then_inc(acc_done, 1)
                    u += 1
                for m2 in range(M2):
                    pe.wait_ge(acc_read, NO + USES * r + M1 + m2 + 1)
                    last = pe.matmul(ps_acc[0:1, u % 2, 0:n], w3[:, m2:m2 + 1], h2[:, m2, b0:bn],
                                     start=(m2 == 0), stop=(m2 == M2 - 1))
                last.then_inc(acc_done, 1)

            turn_ids()
            take = {"ids": broadcast_ids, "look": look_up, "turn": turn_rows, "gram": gram, "zt": turn_products,
                    "dense": first_layer, "later": later_layers}
            for what, *which in steps:
                if what in take:
                    take[what](*which)

        @block.vector
        def _(dve):
            def low_part(n):
                dve.wait_ge(hi_ready, n + 1)
                if n >= PR:
                    dve.wait_ge(acc_done, n - PR + 1)
                dve.tensor_tensor(lo[0:VP, n % PR], table[0:VP, n % TR], hi[0:VP, n % PR].bitcast(F32),
                                  ALU.subtract).then_inc(lo_ready, 1)

            def make_hot(n):
                dve.wait_ge(id_row_ready, n + 1)
                if n == 0:
                    dve.wait_ge(cst_in, 16)
                if n >= 2:
                    dve.wait_ge(acc_done, n - 1)
                for q in range(VQ):
                    last = dve.tensor_scalar(hot[0:VP, n % 2, q, :], id_row[0:VP, n % IR, :], row_no[0:VP, q:q + 1], None,
                                             ALU.is_equal)
                last.then_inc(hot_ready, 1)

            def copy_rows(c, i):
                t = c * NB + i
                if copier(t) == 0:
                    dve.wait_ge(emb_tr, t + 1)
                    emb_t_copy(dve.tensor_copy, c, i).then_inc(emb_read[0], 1)

            def products(c):
                dve.wait_ge(gram_done, c + 1)
                if c >= 2:
                    dve.wait_ge(zc_act, c - 1)
                src = ps_gram[:, :, 0:spb * NF].rearrange("p h (s j) -> p j h s", j=NF)
                dve.transpose(z[:, c % 2, 1:NF, :], src[:, 1:NF]).then_inc(z_ready, 1)
                dve.wait_ge(z_ready, c + 1)
                for n in mine["dve"]:
                    last = compact(dve.tensor_copy, c, n)
                last.then_inc(zc_dve, 1)

            def copy_zt(c):
                dve.wait_ge(zt_done, c + 1)
                dve.tensor_copy(zt[:, :, c * P:(c + 1) * P],
                                ps_z[:, 0:KT * P].rearrange("p (g b) -> p g b", b=P)).then_inc(zt_ready, 1)

            dve.memset(ps_z[:], 0.0).then_inc(init_done, 1)
            dve.wait_ge(ids_in, 16)
            dve.tensor_copy(ids_f[:], ids_sb[:]).then_inc(ids_f_ready, 1)
            dve.wait_ge(cst_in, 16)
            dve.tensor_copy(ident16[:], ident[0:NF, 0:NF])
            dve.wait_ge(ids_t_done, 1)
            dve.tensor_scalar(ids_t[:], ps_z[0:NF, 0:B], F16_EXACT, None, ALU.min).then_inc(ids_t_ready, 1)
            dve.memset(ps_gram[:], 0.0).then_inc(init_done, 1)
            take = {"parts": low_part, "hot": make_hot, "turn": copy_rows, "products": products, "zt": copy_zt}
            for what, *which in steps:
                if what in take:
                    take[what](*which)

        @block.scalar
        def _(act):
            def copy(out, in_):
                return act.activation(out, in_, ACT.Copy)

            def high_part(n):
                act.wait_ge(table_in[n], 32)
                if n >= PR:
                    act.wait_ge(acc_done, n - PR + 1)
                copy(hi[0:VP, n % PR], table[0:VP, n % TR]).then_inc(hi_ready, 1)

            def copy_id_row(n):
                act.wait_ge(bcast_done, n + 1)
                if n >= IR:
                    act.wait_ge(hot_ready, n - IR + 1)
                copy(id_row[:, n % IR, :], ps_z[:, 0:B]).then_inc(id_row_ready, 1)

            def looked_up(n):
                act.wait_ge(acc_done, n + 1)
                copy(emb_t[:, :, one_hot[n]], ps_acc[:, n % 2, 0:B]).then_inc(acc_read, 1)

            def copy_rows(c, i):
                t = c * NB + i
                if copier(t) == 1:
                    act.wait_ge(emb_tr, t + 1)
                    emb_t_copy(copy, c, i).then_inc(emb_read[1], 1)

            def compact_products(c):
                act.wait_ge(z_ready, c + 1)
                for n in mine["act"]:
                    last = compact(copy, c, n)
                last.then_inc(zc_act, 1)

            def first_layer(r):
                b0, bn = ranges[r]
                n = bn - b0
                u = NO + USES * r
                if r == 0:
                    act.wait_ge(w_in, weight_count)
                for m in range(M1):
                    act.wait_ge(acc_done, u + 1)
                    act.activation(h1[:, m, b0:bn], ps_acc[:, u % 2, 0:n], ACT.Relu,
                                   bias=b1[:, m:m + 1]).then_inc(acc_read, 1)
                    u += 1

            def later_layers(r):
                b0, bn = ranges[r]
                n = bn - b0
                u = NO + USES * r + M1
                for m2 in range(M2):
                    act.wait_ge(acc_done, u + 1)
                    act.activation(h2[:, m2, b0:bn], ps_acc[:, u % 2, 0:n], ACT.Relu,
                                   bias=b2[:, m2:m2 + 1]).then_inc(acc_read, 1)
                    u += 1
                act.wait_ge(acc_done, u + 1)
                copy(y_row[0:1, b0:bn], ps_acc[0:1, u % 2, 0:n]).then_inc(acc_read, 1)

            act.dma_start(cst[:], consts).then_inc(cst_in, 16)
            take = {"ids": copy_id_row, "parts": high_part, "look": looked_up, "turn": copy_rows,
                    "products": compact_products, "dense": first_layer, "later": later_layers}
            for what, *which in steps:
                if what in take:
                    take[what](*which)


N_TABLES = 27
_INS = ["dense_ctx", "ids"] + [f"tbl_{f}" for f in range(N_TABLES)] + ["W_top1", "b_top1", "W_top2", "b_top2", "W_top3"]


def kernel(**inputs):
    import numpy as _np
    import concourse.bacc as _bacc
    from concourse import mybir as _mybir
    from concourse.bass_utils import run_bass_kernel_spmd as _run

    nc = _bacc.Bacc("TRN2", target_bir_lowering=False, num_devices=1)
    arrays, aps = {}, {}

    def give(name, a):
        arrays[f"in_{name}"] = a
        aps[name] = nc.dram_tensor(f"in_{name}", a.shape, _mybir.dt.from_np(a.dtype), kind="ExternalInput").ap()

    for name in _INS:
        give(name, _np.ascontiguousarray(inputs[name]))
    give("consts", _np.concatenate([_np.eye(P, dtype=_np.float32),
                                    _np.arange(P * VQ, dtype=_np.float32).reshape(P, VQ)], axis=1))
    batch = inputs["ids"].shape[0]
    y = nc.dram_tensor("out_y", (batch, 1), _mybir.dt.float32, kind="ExternalOutput").ap()
    build(nc, aps["dense_ctx"], aps["ids"], [aps[f"tbl_{f}"] for f in range(N_TABLES)], aps["W_top1"], aps["b_top1"],
          aps["W_top2"], aps["b_top2"], aps["W_top3"], aps["consts"], y)
    r = _run(nc, [arrays], core_ids=[0])
    return r.results[0]["out_y"]
```

```python
from collections import namedtuple
from contextlib import ExitStack

import numpy as np
import concourse.bass as bass
from concourse import mybir

F32 = mybir.dt.float32
F16 = mybir.dt.float16
BF16 = mybir.dt.bfloat16
F32R = mybir.dt.float32r
U32 = mybir.dt.uint32
ALU = mybir.AluOpType
ACT = mybir.ActivationFunctionType

P = 128
Q = 32
NQ = P // Q
BANK = 512
ONE_HOT_VOCAB = 1000
F16_EXACT = 2048.0
MAX_ONE_HOT = 10
PART_FROM = 1
VP = 125
VQ = ONE_HOT_VOCAB // VP
IW = 2
TR, PR, IR, ER = 3, 3, 3, 3
ACT_FIRST = 10
WARM = (20, 9, 14)
SHARES = (0.6, 1)
FULL_DMA = VP // 16 * 16


Part = namedtuple("Part", "rows dve_blocks act_blocks tiles")


def pair_blocks(nf, spare):
    blocks, j = [], 1
    while j < nf:
        rows = min(2, nf - j)
        if rows + 1 <= nf - j and spare - 3 >= (nf - j - 3 + 1) // 2:
            rows = 3
        spare -= rows * (rows - 1) // 2
        blocks.append((j, j + rows, j + rows - 1))
        j += rows
    assert spare >= 0
    return blocks


def runs(features):
    out = []
    for i, f in enumerate(features):
        if out and out[-1][1] + out[-1][2] == f:
            out[-1][2] += 1
        else:
            out.append([i, f, 1])
    return out


def build(nc, dense_ctx, ids, tables, w_top1, b_top1, w_top2, b_top2, w_top3, consts, y):
    B, NF = ids.shape
    D = tables[0].shape[1]
    ND = dense_ctx.shape[1]
    N1, N2 = w_top1.shape[1], w_top2.shape[1]
    M1, M2 = N1 // P, N2 // P
    CH = B // P
    assert D == P and NF <= Q

    one_hot = [f for f in range(NF) if tables[f].shape[0] == ONE_HOT_VOCAB][-MAX_ONE_HOT:]
    NO = len(one_hot)
    look_from = [0] * (NO - 1) + [PART_FROM * P]
    gathered = [f for f in range(NF) if f not in one_hot[:-1]]
    gathered.sort(key=lambda f: f == one_hot[-1])
    NG = len(gathered)
    batches = [[gathered[i:i + BANK // P] for i in range(0, NG, BANK // P)] for c in range(CH)]
    for c in range(PART_FROM, CH):
        del batches[c][-1][-1]
    NB = len(batches[0])
    assert all(all(b) for b in batches)
    pairs = NF * (NF - 1) // 2
    KT = -(-(pairs + ND) // P)
    blocks = pair_blocks(NF, KT * P - pairs - ND)
    starts = [sum((j1 - j0) * w for j0, j1, w in blocks[:n]) for n in range(len(blocks) + 1)]
    K1 = starts[-1] + ND
    tiles = [(g * P, min((g + 1) * P, K1)) for g in range(KT)]
    spb = Q // 2
    assert spb * NF <= BANK and KT * P <= BANK and len(tiles) == KT

    with ExitStack() as ctx:
        def sb(name, shape, dt=F32):
            return ctx.enter_context(nc.sbuf_tensor(name, shape, dt))

        def psum(name, shape):
            return ctx.enter_context(nc.psum_tensor(name, shape, F32))

        def sem(name):
            return ctx.enter_context(nc.semaphore(name))

        cst = sb("cst", [P, P + VQ])
        ident, row_no = cst[:, 0:P], cst[:, P:P + VQ]
        ids_sb = sb("ids_sb", [P, CH, NF], ids.dtype)
        ids_f = sb("ids_f", [P, CH, NF])
        ids_t = sb("ids_t", [NF, B], F16)
        ident16 = sb("ident16", [NF, NF], F16)
        warm = sb("warm", [P, P], BF16)
        emb = sb("emb", [P, ER, NG, D])
        emb_t = sb("emb_t", [P, B, NF])
        table = sb("table", [P, TR, VQ, D])
        hi = sb("hi", [P, PR, VQ, D], F32R)
        lo = sb("lo", [P, PR, VQ, D], F32R)
        id_row = sb("id_row", [P, IR, IW, B])
        hot = sb("hot", [P, 2, VQ, B], F32R)
        z = sb("z", [P, 2, NF, Q])
        zc = sb("zc", [P, CH, KT * P])
        zt = sb("zt", [P, KT, B])
        w1 = sb("w1", [P, KT, N1])
        w2 = sb("w2", [P, M1, N2])
        w3 = sb("w3", [P, M2])
        b1 = sb("b1", [P, M1])
        b2 = sb("b2", [P, M2])
        h1 = sb("h1", [P, M1, B])
        h2 = sb("h2", [P, M2, B])
        y_row = sb("y_row", [1, B])

        ps_emb = psum("ps_emb", [P, 2, BANK])
        ps_gram = psum("ps_gram", [P, 2, BANK])
        ps_z = psum("ps_z", [P, BANK])
        ps_bc = psum("ps_bc", [P, BANK])
        ps_acc = psum("ps_acc", [P, 2, BANK])

        ids_in = sem("ids_in")
        cst_in = sem("cst_in")
        dense_in = sem("dense_in")
        w_in = sem("w_in")
        pieces = [[(0, VQ // 2), (VQ // 2, VQ)] if n == 0 else [(0, VQ)] for n in range(NO)]
        groups = [[(q, q + 1) for q in range(VQ)] if n == 0 else [(q, q + IW) for q in range(0, VQ, IW)] for n in range(NO)]

        def count(cut, n):
            return sum(len(c) for c in cut[:n])

        table_in = [[sem(f"table_in{n}_{i}") for i in range(len(pieces[n]))] for n in range(NO)]
        rows_in = [[sem(f"rows_in{c}_{i}") for i in range(NB)] for c in range(CH)]
        y_out = sem("y_out")
        w1_zero = sem("w1_zero")
        init_done = sem("init_done")
        ids_f_ready = sem("ids_f_ready")
        ids_t_done = sem("ids_t_done")
        ids_t_ready = sem("ids_t_ready")
        bcast_done = sem("bcast_done")
        id_row_ready = sem("id_row_ready")
        hi_ready = sem("hi_ready")
        lo_ready = sem("lo_ready")
        hot_ready = sem("hot_ready")
        hot_used = sem("hot_used")
        acc_done = sem("acc_done")
        acc_read = sem("acc_read")
        emb_tr = sem("emb_tr")
        emb_read = [sem("emb_read_dve"), sem("emb_read_act")]
        gram_done = sem("gram_done")
        z_ready = sem("z_ready")
        zc_dve = sem("zc_dve")
        zc_act = sem("zc_act")
        zt_done = sem("zt_done")
        zt_ready = sem("zt_ready")

        ranges = [(c * P, (c + 1) * P) for c in range(CH)]
        edge = sum(at < P for at in starts[:-1])

        def part(a, b, share, of_tiles):
            own = a + round((b - a) * share)
            return Part((blocks[a][0], blocks[b - 1][1]), range(a, own), range(own, b), of_tiles)

        whole = [part(0, len(blocks), 2 / 3, range(KT))]
        halves = [part(0, edge, SHARES[0], range(0, 1)), part(edge, len(blocks), SHARES[1], range(1, KT))]
        parts = [halves if c == CH - 1 else whole for c in range(CH)]

        w1_rows = []
        for at, (j0, j1, w) in zip(starts, blocks):
            w1_rows += [(at + (j - j0) * w, j * (j - 1) // 2, j) for j in range(j0, j1)]
        w1_rows.append((starts[-1], pairs, ND))
        w1_rows = [(max(at, a), first + max(at, a) - at, min(at + n, b) - max(at, a))
                   for at, first, n in w1_rows for a, b in tiles if at < b and at + n > a]

        steps = []
        units, all_tiles = range(M1), range(KT)

        def prepare(n, what):
            if n < NO:
                steps.append((what, n))

        def turns(n):
            for _ in range(n):
                t = sum(s[0] == "turn" for s in steps)
                steps.append(("turn", t // NB, t % NB))

        steps += [("parts", 0), ("ids", 0), ("hot", 0), ("ids", 1), ("parts", 1), ("hot", 1)]
        for n in range(NO):
            prepare(n + 2, "parts")
            steps.append(("look", n))
            prepare(n + 2, "ids")
            prepare(n + 2, "hot")
            turns(1)
        turns(2 * NB - NO)
        steps += [("gram", 0), ("products", 0, 0), ("compact", 0, 0)]
        turns(2)
        steps += [("gram", 1), ("zt", 0, 0), ("products", 1, 0)]
        turns(1)
        steps += [("first", 0, units, all_tiles), ("compact", 1, 0), ("second", 0, 0), ("second", 0, 1), ("zt", 1, 0),
                  ("last", 0), ("first", 1, units, all_tiles)]
        turns(2)
        steps += [("second", 1, 0), ("gram", 2), ("products", 2, 0), ("second", 1, 1), ("compact", 2, 0)]
        turns(1)
        steps += [("last", 1), ("zt", 2, 0)]
        turns(2)
        steps += [("first", 2, units[:2], all_tiles)]
        turns(1)
        steps += [("first", 2, units[2:3], all_tiles)]
        turns(1)
        steps += [("first", 2, units[3:], all_tiles)]
        steps += [("gram", 3), ("products", 3, 0), ("products", 3, 1), ("compact", 3, 0), ("second", 2, 0),
                  ("second", 2, 1), ("zt", 3, 0), ("zt", 3, 1), ("compact", 3, 1), ("first", 3, units, all_tiles[:1]),
                  ("first", 3, units, all_tiles[1:]), ("second", 3, 0), ("second", 3, 1), ("last", 2), ("last", 3)]
        assert steps.count(("turn", CH - 1, NB - 1)) == 1

        numbered = []
        for what, *which in steps:
            if what in ("look", "second", "last"):
                numbered.append((what, *which))
            elif what == "first" and KT - 1 in which[2]:
                numbered += [("first", which[0], m) for m in which[1]]
        number = {key: u for u, key in enumerate(numbered)}
        assert [number["look", n] for n in range(NO)] == list(range(NO))

        def copier(t):
            return 1 if t < ACT_FIRST or t % 2 else 0

        def copies(t, who):
            return sum(copier(x) == who for x in range(t))

        weight_count = 16 * (len(w1_rows) + 4)

        block = ctx.enter_context(nc.Block())

        @block.sync
        def _(sp):
            sp.dma_start(ids_sb[:], ids.rearrange("(c p) f -> p c f", p=P)).then_inc(ids_in, 16)
            for n, f in enumerate(one_hot):
                if n >= TR:
                    sp.wait_ge(lo_ready, count(pieces, n - TR + 1))
                src = tables[f].rearrange("(p q) d -> p q d", q=VQ)
                for i, (q0, q1) in enumerate(pieces[n]):
                    for a, b in ((0, FULL_DMA), (FULL_DMA, VP)):
                        sp.dma_start(table[a:b, n % TR, q0:q1], src[a:b, q0:q1]).then_inc(table_in[n][i], 16)
                if n >= TR:
                    sp.wait_ge(w1_zero, 1)
                    for at, first, rows in w1_rows[n - TR::NO - TR]:
                        g, p0 = at // P, at % P
                        sp.dma_start(w1[p0:p0 + rows, g, :], w_top1[first:first + rows, :]).then_inc(w_in, 16)
            sp.dma_start(zc[:, :, starts[-1]:K1], dense_ctx.rearrange("(c p) e -> p c e", p=P)
                         ).then_inc(dense_in, 16)
            with nc.allow_non_contiguous_dma(reason="biases and last weights, one value per partition"):
                sp.dma_start(b1[:], b_top1.rearrange("(m p) -> p m", p=P)).then_inc(w_in, 16)
                sp.dma_start(b2[:], b_top2.rearrange("(m p) -> p m", p=P)).then_inc(w_in, 16)
                sp.dma_start(w3[:], w_top3.rearrange("(m p) o -> p (m o)", p=P)).then_inc(w_in, 16)
            sp.dma_start(w2[:], w_top2.rearrange("(m p) n -> p m n", p=P)).then_inc(w_in, 16)
            sp.wait_ge(acc_read, len(numbered))
            sp.dma_start(y.rearrange("b o -> o b"), y_row[:]).then_inc(y_out, 16)
            sp.wait_ge(y_out, 16)

        @block.gpsimd
        def _(pool):
            pool.memset(w1[:], 0.0).then_inc(w1_zero, 1)
            pool.wait_ge(ids_in, 16)
            for c in range(CH):
                for i, batch in enumerate(batches[c]):
                    if c >= ER:
                        pool.wait_ge(emb_tr, (c - ER) * NB + i + 1)
                    for s, f in enumerate(batch):
                        index = ids_sb[:, c, f:f + 1].bitcast(U32)
                        pool.indirect_dma_start(emb[:, c % ER, i * (BANK // P) + s, :], None, tables[f],
                                                bass.IndirectOffsetOnAxis(ap=index, axis=0)
                                                ).then_inc(rows_in[c][i], 16)

        def emb_t_copy(eng_copy, c, i):
            src = ps_emb[:, (c * NB + i) % 2, :].rearrange("p (f b) -> p b f", b=P)
            for at, f, n in runs(batches[c][i]):
                last = eng_copy(emb_t[:, c * P:(c + 1) * P, f:f + n], src[:, :, at:at + n])
            return last

        def compact(eng_copy, c, n):
            j0, j1, w = blocks[n]
            return eng_copy(zc[:, c, starts[n]:starts[n + 1]].rearrange("p (j i) -> p j i", i=w), z[:, c % 2, j0:j1, 0:w])

        def first_sum(r, m):
            n = ranges[r][1] - ranges[r][0]
            if r < len(ranges) - 1:
                return ps_acc[:, number["first", r, m] % 2, 0:n]
            return (ps_emb, ps_gram)[m // 2][:, m % 2, 0:n]

        @block.tensor
        def _(pe):
            def keep_warm(n):
                for _ in range(n):
                    pe.matmul(ps_emb[:, 0, 0:P], warm[:], warm[:], start=True, stop=True)

            def turn_ids():
                pe.wait_ge(cst_in, 16)
                pe.wait_ge(init_done, 2)
                pe.wait_ge(ids_f_ready, 1)
                for c in range(CH):
                    last = pe.transpose(ps_z[0:NF, c * P:(c + 1) * P], ids_f[:, c, :], ident)
                last.then_inc(ids_t_done, 1)

            def broadcast_ids(n):
                pe.wait_ge(ids_t_ready, 1)
                if n >= 2:
                    pe.wait_ge(id_row_ready, IW * (n - 1))
                f = one_hot[n]
                pe.matmul((ps_z, ps_bc)[n % 2][:, 0:B], ident16[:, f:f + 1].to_broadcast([NF, P]), ids_t[:, :],
                          start=True, stop=True).then_inc(bcast_done, 1)

            def look_up(n):
                b0 = look_from[n]
                if n == 0:
                    keep_warm(WARM[2])
                if n >= 2:
                    pe.wait_ge(acc_read, n - 1)
                for j, (q0, q1) in enumerate(groups[n]):
                    for i, (piece, _) in enumerate(pieces[n]):
                        if q0 == piece:
                            pe.wait_ge(lo_ready, count(pieces, n) + i + 1)
                    pe.wait_ge(hot_ready, count(groups, n) + j + 1)
                    for q in range(q0, q1):
                        for part in (hi, lo):
                            last = pe.matmul(ps_acc[:, n % 2, b0:B], part[0:VP, n % PR, q, :], hot[0:VP, n % 2, q, b0:B],
                                             start=(q == 0 and part is hi), stop=(q == VQ - 1 and part is lo))
                    if q1 % IW == 0 and q1 < VQ:
                        last.then_inc(hot_used, 1)
                last.then_inc(acc_done, 1)

            def turn_rows(c, i):
                t = c * NB + i
                pe.wait_ge(cst_in, 16)
                pe.wait_ge(rows_in[c][i], 16 * len(batches[c][i]))
                if t >= 2:
                    pe.wait_ge(emb_read[copier(t - 2)], copies(t - 1, copier(t - 2)))
                for s in range(len(batches[c][i])):
                    last = pe.transpose(ps_emb[:, t % 2, s * P:(s + 1) * P], emb[:, c % ER, i * (BANK // P) + s, :], ident)
                last.then_inc(emb_tr, 1)

            def gram(c):
                if c == 0:
                    pe.wait_ge(init_done, 3)
                else:
                    pe.wait_ge(z_ready, c)
                if c <= PART_FROM:
                    pe.wait_ge(acc_read, NO if c == PART_FROM else NO - 1)
                for who in range(2):
                    if copies((c + 1) * NB, who):
                        pe.wait_ge(emb_read[who], copies((c + 1) * NB, who))
                for s in range(Q):
                    for k in range(NQ):
                        e = emb_t[:, c * P + k * Q + s, :]
                        out = ps_gram[k * Q:k * Q + NF, s // spb, s % spb * NF:(s % spb + 1) * NF]
                        last = pe.matmul(out, e, e, start=True, stop=True, tile_position=(0, k * Q))
                last.then_inc(gram_done, 1)

            def turn_products(c, i):
                pe.wait_ge(zc_dve, c + i + 1)
                pe.wait_ge(zc_act, c + 1)
                if c == 0:
                    pe.wait_ge(dense_in, 16)
                    pe.wait_ge(id_row_ready, IW * NO)
                elif i == 0:
                    pe.wait_ge(zt_ready, KT * c)
                for g in parts[c][i].tiles:
                    a, b = tiles[g]
                    last = pe.transpose((ps_z, ps_bc)[i][0:b - a, g * P:(g + 1) * P], zc[:, c, a:b], ident)
                last.then_inc(zt_done, 1)

            def first_layer(r, of_units, of_tiles):
                b0, bn = ranges[r]
                if r == 0:
                    pe.wait_ge(w_in, weight_count)
                for m in of_units:
                    for g in of_tiles:
                        if m == of_units[0]:
                            pe.wait_ge(zt_ready, KT * r + g + 1)
                        if g == 0 and r < len(ranges) - 1:
                            pe.wait_ge(acc_read, number["first", r, m] - 1)
                        a, b = tiles[g]
                        last = pe.matmul(first_sum(r, m), w1[0:b - a, g, m * P:(m + 1) * P], zt[0:b - a, g, b0:bn],
                                         start=(g == 0), stop=(g == KT - 1))
                    if g == KT - 1:
                        last.then_inc(acc_done, 1)

            def second_layer(r, m2):
                b0, bn = ranges[r]
                n = bn - b0
                u = number["second", r, m2]
                if r < len(ranges) - 1:
                    pe.wait_ge(acc_read, u - 1)
                for m in range(M1):
                    if m2 == 0:
                        pe.wait_ge(acc_read, number["first", r, m] + 1)
                    last = pe.matmul(ps_acc[:, u % 2, 0:n], w2[:, m, m2 * P:(m2 + 1) * P], h1[:, m, b0:bn],
                                     start=(m == 0), stop=(m == M1 - 1))
                last.then_inc(acc_done, 1)

            def last_layer(r):
                b0, bn = ranges[r]
                n = bn - b0
                u = number["last", r]
                pe.wait_ge(acc_read, u - 1)
                for m2 in range(M2):
                    pe.wait_ge(acc_read, number["second", r, m2] + 1)
                    last = pe.matmul(ps_acc[0:1, u % 2, 0:n], w3[:, m2:m2 + 1], h2[:, m2, b0:bn],
                                     start=(m2 == 0), stop=(m2 == M2 - 1))
                last.then_inc(acc_done, 1)

            pe.wait_ge(init_done, 1)
            keep_warm(WARM[0])
            turn_ids()
            keep_warm(WARM[1])
            take = {"ids": broadcast_ids, "look": look_up, "turn": turn_rows, "gram": gram, "zt": turn_products,
                    "first": first_layer, "second": second_layer, "last": last_layer}
            for what, *which in steps:
                if what in take:
                    take[what](*which)

        @block.vector
        def _(dve):
            def low_part(n):
                if n >= PR:
                    dve.wait_ge(acc_done, n - PR + 1)
                for i, (q0, q1) in enumerate(pieces[n]):
                    dve.wait_ge(hi_ready, count(pieces, n) + i + 1)
                    dve.tensor_tensor(lo[0:VP, n % PR, q0:q1], table[0:VP, n % TR, q0:q1],
                                      hi[0:VP, n % PR, q0:q1].bitcast(F32), ALU.subtract).then_inc(lo_ready, 1)

            def make_hot(n):
                b0 = look_from[n]
                if n == 0:
                    dve.wait_ge(cst_in, 16)
                for j, (q0, q1) in enumerate(groups[n]):
                    k0, k1 = q0 % IW, (q1 - 1) % IW + 1
                    if j < 2:
                        dve.wait_ge(id_row_ready, IW * n + k1)
                    if n >= 2:
                        if q1 < VQ:
                            dve.wait_ge(hot_used, (VQ // IW - 1) * (n - 2) + q1 // IW)
                        else:
                            dve.wait_ge(acc_done, n - 1)
                    dve.tensor_scalar(hot[0:VP, n % 2, q0:q1, b0:B], id_row[0:VP, n % IR, k0:k1, b0:B],
                                      row_no[0:VP, q0 - k0:q0 - k0 + 1], None, ALU.is_equal).then_inc(hot_ready, 1)

            def copy_rows(c, i):
                t = c * NB + i
                if copier(t) == 0:
                    dve.wait_ge(emb_tr, t + 1)
                    emb_t_copy(dve.tensor_copy, c, i).then_inc(emb_read[0], 1)

            def products(c, i):
                j0, j1 = parts[c][i].rows
                if i == 0:
                    dve.wait_ge(gram_done, c + 1)
                    if c >= 2:
                        dve.wait_ge(zc_act, c - 1)
                src = ps_gram[:, :, 0:spb * NF].rearrange("p h (s j) -> p j h s", j=NF)
                dve.transpose(z[:, c % 2, j0:j1, :], src[:, j0:j1]).then_inc(z_ready, 1)
                dve.wait_ge(z_ready, c + i + 1)
                for n in parts[c][i].dve_blocks:
                    last = compact(dve.tensor_copy, c, n)
                last.then_inc(zc_dve, 1)

            def copy_zt(c, i):
                dve.wait_ge(zt_done, c + i + 1)
                for g in parts[c][i].tiles:
                    a, b = tiles[g]
                    dve.tensor_copy(zt[0:b - a, g, c * P:(c + 1) * P], (ps_z, ps_bc)[i][0:b - a, g * P:(g + 1) * P]
                                    ).then_inc(zt_ready, 1)

            dve.memset(warm[:], 0.0).then_inc(init_done, 1)
            dve.memset(ps_z[:], 0.0).then_inc(init_done, 1)
            dve.memset(ps_gram[:], 0.0).then_inc(init_done, 1)
            dve.wait_ge(ids_in, 16)
            dve.tensor_copy(ids_f[:], ids_sb[:]).then_inc(ids_f_ready, 1)
            dve.wait_ge(cst_in, 16)
            dve.tensor_copy(ident16[:], ident[0:NF, 0:NF])
            dve.wait_ge(ids_t_done, 1)
            dve.tensor_scalar(ids_t[:], ps_z[0:NF, 0:B], F16_EXACT, None, ALU.min).then_inc(ids_t_ready, 1)
            take = {"parts": low_part, "hot": make_hot, "turn": copy_rows, "products": products, "zt": copy_zt}
            for what, *which in steps:
                if what in take:
                    take[what](*which)

        @block.scalar
        def _(act):
            def copy(out, in_):
                return act.activation(out, in_, ACT.Copy)

            def high_part(n):
                if n >= PR:
                    act.wait_ge(acc_done, n - PR + 1)
                for i, (q0, q1) in enumerate(pieces[n]):
                    act.wait_ge(table_in[n][i], 32)
                    copy(hi[0:VP, n % PR, q0:q1], table[0:VP, n % TR, q0:q1]).then_inc(hi_ready, 1)

            def copy_id_row(n):
                act.wait_ge(bcast_done, n + 1)
                if n >= IR:
                    act.wait_ge(hot_ready, count(groups, n - IR + 1))
                for k in range(IW):
                    act.activation(id_row[:, n % IR, k, :], (ps_z, ps_bc)[n % 2][:, 0:B], ACT.Copy, bias=float(-k)
                                   ).then_inc(id_row_ready, 1)

            def looked_up(n):
                act.wait_ge(acc_done, n + 1)
                b0 = look_from[n]
                copy(emb_t[:, b0:B, one_hot[n]], ps_acc[:, n % 2, b0:B]).then_inc(acc_read, 1)

            def copy_rows(c, i):
                t = c * NB + i
                if copier(t) == 1:
                    act.wait_ge(emb_tr, t + 1)
                    emb_t_copy(copy, c, i).then_inc(emb_read[1], 1)

            def compact_products(c, i):
                if not parts[c][i].act_blocks:
                    return
                act.wait_ge(z_ready, c + i + 1)
                for n in parts[c][i].act_blocks:
                    last = compact(copy, c, n)
                last.then_inc(zc_act, 1)

            def first_layer(r, of_units, of_tiles):
                b0, bn = ranges[r]
                if KT - 1 not in of_tiles:
                    return
                if r == 0:
                    act.wait_ge(w_in, weight_count)
                for m in of_units:
                    act.wait_ge(acc_done, number["first", r, m] + 1)
                    act.activation(h1[:, m, b0:bn], first_sum(r, m), ACT.Relu, bias=b1[:, m:m + 1]).then_inc(acc_read, 1)

            def second_layer(r, m2):
                b0, bn = ranges[r]
                n = bn - b0
                u = number["second", r, m2]
                act.wait_ge(acc_done, u + 1)
                act.activation(h2[:, m2, b0:bn], ps_acc[:, u % 2, 0:n], ACT.Relu,
                               bias=b2[:, m2:m2 + 1]).then_inc(acc_read, 1)

            def last_layer(r):
                b0, bn = ranges[r]
                n = bn - b0
                u = number["last", r]
                act.wait_ge(acc_done, u + 1)
                copy(y_row[0:1, b0:bn], ps_acc[0:1, u % 2, 0:n]).then_inc(acc_read, 1)

            act.dma_start(cst[:], consts).then_inc(cst_in, 16)
            take = {"ids": copy_id_row, "parts": high_part, "look": looked_up, "turn": copy_rows,
                    "compact": compact_products, "first": first_layer, "second": second_layer, "last": last_layer}
            for what, *which in steps:
                if what in take:
                    take[what](*which)


N_TABLES = 27
_INS = ["dense_ctx", "ids"] + [f"tbl_{f}" for f in range(N_TABLES)] + ["W_top1", "b_top1", "W_top2", "b_top2", "W_top3"]


def kernel(**inputs):
    import numpy as _np
    import concourse.bacc as _bacc
    from concourse import mybir as _mybir
    from concourse.bass_utils import run_bass_kernel_spmd as _run

    nc = _bacc.Bacc("TRN2", target_bir_lowering=False, num_devices=1)
    arrays, aps = {}, {}

    def give(name, a):
        arrays[f"in_{name}"] = a
        aps[name] = nc.dram_tensor(f"in_{name}", a.shape, _mybir.dt.from_np(a.dtype), kind="ExternalInput").ap()

    for name in _INS:
        give(name, _np.ascontiguousarray(inputs[name]))
    give("consts", _np.concatenate([_np.eye(P, dtype=_np.float32),
                                    _np.arange(P * VQ, dtype=_np.float32).reshape(P, VQ)], axis=1))
    batch = inputs["ids"].shape[0]
    y = nc.dram_tensor("out_y", (batch, 1), _mybir.dt.float32, kind="ExternalOutput").ap()
    build(nc, aps["dense_ctx"], aps["ids"], [aps[f"tbl_{f}"] for f in range(N_TABLES)], aps["W_top1"], aps["b_top1"],
          aps["W_top2"], aps["b_top2"], aps["W_top3"], aps["consts"], y)
    r = _run(nc, [arrays], core_ids=[0])
    return r.results[0]["out_y"]
```
